# Optimizing a Trainium2 kernel written in Bass

```python
import numpy as np
import jax
import jax.numpy as jnp

def _softmax(x, axis=-1):
    return jax.nn.softmax(x, axis=axis)

def _gelu(x):
    return jax.nn.gelu(x, approximate=True)

def _silu(x):
    return jax.nn.silu(x)

def _sigmoid(x):
    return jax.nn.sigmoid(x)

def _layernorm(x, axis=-1, eps=1e-05):
    m = jnp.mean(x, axis=axis, keepdims=True)
    v = jnp.var(x, axis=axis, keepdims=True)
    return (x - m) / jnp.sqrt(v + eps)

def _scatter_add(tgt, idx, src, axis=0):
    return tgt.at[idx].add(src)

def _segment_sum(src, seg, n):
    return jax.ops.segment_sum(src, seg, n)
kernel_name = 'mk_dlrm_tower_d1_rec_r8_b14fba'

def setup_inputs(seed: int=0):
    np.random.seed(seed)
    _w = jnp.asarray

    def _rec_inputs():
        import jax
        import jax.numpy as jnp
        _tk = jax.random.key(seed)
        dense_ctx = jax.random.normal(jax.random.fold_in(_tk, 190), (2048, 16), jnp.float32)
        ids = jnp.stack([jax.random.randint(jax.random.fold_in(_tk, 200 + f), (2048,), 0, v, jnp.int32) for f, v in enumerate([12500, 12500, 12500, 1250, 12500, 12500, 12500, 125000, 12500, 1250, 1000, 1000, 1250, 1000, 1250, 1250, 1250, 12500, 1000, 12500, 12500, 125000, 1000, 1250, 1000, 1250, 1000, 1000, 12500, 12500, 1000, 12500])], axis=1)
        tbl_0 = 0.05 * jax.random.normal(jax.random.fold_in(_tk, 500 + 0), (12500, 64), jnp.float32)
        tbl_1 = 0.05 * jax.random.normal(jax.random.fold_in(_tk, 500 + 1), (12500, 64), jnp.float32)
        tbl_2 = 0.05 * jax.random.normal(jax.random.fold_in(_tk, 500 + 2), (12500, 64), jnp.float32)
        tbl_3 = 0.05 * jax.random.normal(jax.random.fold_in(_tk, 500 + 3), (1250, 64), jnp.float32)
        tbl_4 = 0.05 * jax.random.normal(jax.random.fold_in(_tk, 500 + 4), (12500, 64), jnp.float32)
        tbl_5 = 0.05 * jax.random.normal(jax.random.fold_in(_tk, 500 + 5), (12500, 64), jnp.float32)
        tbl_6 = 0.05 * jax.random.normal(jax.random.fold_in(_tk, 500 + 6), (12500, 64), jnp.float32)
        tbl_7 = 0.05 * jax.random.normal(jax.random.fold_in(_tk, 500 + 7), (125000, 64), jnp.float32)
        tbl_8 = 0.05 * jax.random.normal(jax.random.fold_in(_tk, 500 + 8), (12500, 64), jnp.float32)
        tbl_9 = 0.05 * jax.random.normal(jax.random.fold_in(_tk, 500 + 9), (1250, 64), jnp.float32)
        tbl_10 = 0.05 * jax.random.normal(jax.random.fold_in(_tk, 500 + 10), (1000, 64), jnp.float32)
        tbl_11 = 0.05 * jax.random.normal(jax.random.fold_in(_tk, 500 + 11), (1000, 64), jnp.float32)
        tbl_12 = 0.05 * jax.random.normal(jax.random.fold_in(_tk, 500 + 12), (1250, 64), jnp.float32)
        tbl_13 = 0.05 * jax.random.normal(jax.random.fold_in(_tk, 500 + 13), (1000, 64), jnp.float32)
        tbl_14 = 0.05 * jax.random.normal(jax.random.fold_in(_tk, 500 + 14), (1250, 64), jnp.float32)
        tbl_15 = 0.05 * jax.random.normal(jax.random.fold_in(_tk, 500 + 15), (1250, 64), jnp.float32)
        tbl_16 = 0.05 * jax.random.normal(jax.random.fold_in(_tk, 500 + 16), (1250, 64), jnp.float32)
        tbl_17 = 0.05 * jax.random.normal(jax.random.fold_in(_tk, 500 + 17), (12500, 64), jnp.float32)
        tbl_18 = 0.05 * jax.random.normal(jax.random.fold_in(_tk, 500 + 18), (1000, 64), jnp.float32)
        tbl_19 = 0.05 * jax.random.normal(jax.random.fold_in(_tk, 500 + 19), (12500, 64), jnp.float32)
        tbl_20 = 0.05 * jax.random.normal(jax.random.fold_in(_tk, 500 + 20), (12500, 64), jnp.float32)
        tbl_21 = 0.05 * jax.random.normal(jax.random.fold_in(_tk, 500 + 21), (125000, 64), jnp.float32)
        tbl_22 = 0.05 * jax.random.normal(jax.random.fold_in(_tk, 500 + 22), (1000, 64), jnp.float32)
        tbl_23 = 0.05 * jax.random.normal(jax.random.fold_in(_tk, 500 + 23), (1250, 64), jnp.float32)
        tbl_24 = 0.05 * jax.random.normal(jax.random.fold_in(_tk, 500 + 24), (1000, 64), jnp.float32)
        tbl_25 = 0.05 * jax.random.normal(jax.random.fold_in(_tk, 500 + 25), (1250, 64), jnp.float32)
        tbl_26 = 0.05 * jax.random.normal(jax.random.fold_in(_tk, 500 + 26), (1000, 64), jnp.float32)
        tbl_27 = 0.05 * jax.random.normal(jax.random.fold_in(_tk, 500 + 27), (1000, 64), jnp.float32)
        tbl_28 = 0.05 * jax.random.normal(jax.random.fold_in(_tk, 500 + 28), (12500, 64), jnp.float32)
        tbl_29 = 0.05 * jax.random.normal(jax.random.fold_in(_tk, 500 + 29), (12500, 64), jnp.float32)
        tbl_30 = 0.05 * jax.random.normal(jax.random.fold_in(_tk, 500 + 30), (1000, 64), jnp.float32)
        tbl_31 = 0.05 * jax.random.normal(jax.random.fold_in(_tk, 500 + 31), (12500, 64), jnp.float32)
        _rk = jax.random.fold_in(_tk, 7)
        W_top1 = 0.0441942 * jax.random.normal(jax.random.fold_in(_tk, 801), (512, 512), jnp.float32)
        W_top2 = 0.0441942 * jax.random.normal(jax.random.fold_in(_tk, 802), (512, 256), jnp.float32)
        W_top3 = 0.0625 * jax.random.normal(jax.random.fold_in(_tk, 803), (256, 1), jnp.float32)
        b_top1 = jnp.zeros((512,), jnp.float32)
        b_top2 = jnp.zeros((256,), jnp.float32)
        return (dense_ctx, ids, tbl_0, tbl_1, tbl_2, tbl_3, tbl_4, tbl_5, tbl_6, tbl_7, tbl_8, tbl_9, tbl_10, tbl_11, tbl_12, tbl_13, tbl_14, tbl_15, tbl_16, tbl_17, tbl_18, tbl_19, tbl_20, tbl_21, tbl_22, tbl_23, tbl_24, tbl_25, tbl_26, tbl_27, tbl_28, tbl_29, tbl_30, tbl_31, W_top1, b_top1, W_top2, b_top2, W_top3)
    dense_ctx, ids, tbl_0, tbl_1, tbl_2, tbl_3, tbl_4, tbl_5, tbl_6, tbl_7, tbl_8, tbl_9, tbl_10, tbl_11, tbl_12, tbl_13, tbl_14, tbl_15, tbl_16, tbl_17, tbl_18, tbl_19, tbl_20, tbl_21, tbl_22, tbl_23, tbl_24, tbl_25, tbl_26, tbl_27, tbl_28, tbl_29, tbl_30, tbl_31, W_top1, b_top1, W_top2, b_top2, W_top3 = _rec_inputs()

    def _L0_rec_setup():
        import jax, jax.numpy as jnp
        import numpy as np
        NUM_FIELDS = 32
        key = jax.random.key(seed)
        x = jax.random.normal(key, (2048, NUM_FIELDS, 64), dtype=jnp.float32)
        return {'x': x}
    _L0_rec_all = _L0_rec_setup()
    _L0_rec_in = {k: v for k, v in _L0_rec_all.items() if k in ()}
    del _L0_rec_all
    return {'dense_ctx': dense_ctx, 'ids': ids, 'tbl_0': tbl_0, 'tbl_1': tbl_1, 'tbl_2': tbl_2, 'tbl_3': tbl_3, 'tbl_4': tbl_4, 'tbl_5': tbl_5, 'tbl_6': tbl_6, 'tbl_7': tbl_7, 'tbl_8': tbl_8, 'tbl_9': tbl_9, 'tbl_10': tbl_10, 'tbl_11': tbl_11, 'tbl_12': tbl_12, 'tbl_13': tbl_13, 'tbl_14': tbl_14, 'tbl_15': tbl_15, 'tbl_16': tbl_16, 'tbl_17': tbl_17, 'tbl_18': tbl_18, 'tbl_19': tbl_19, 'tbl_20': tbl_20, 'tbl_21': tbl_21, 'tbl_22': tbl_22, 'tbl_23': tbl_23, 'tbl_24': tbl_24, 'tbl_25': tbl_25, 'tbl_26': tbl_26, 'tbl_27': tbl_27, 'tbl_28': tbl_28, 'tbl_29': tbl_29, 'tbl_30': tbl_30, 'tbl_31': tbl_31, 'W_top1': W_top1, 'b_top1': b_top1, 'W_top2': W_top2, 'b_top2': b_top2, 'W_top3': W_top3}

def reference(dense_ctx, ids, tbl_0, tbl_1, tbl_2, tbl_3, tbl_4, tbl_5, tbl_6, tbl_7, tbl_8, tbl_9, tbl_10, tbl_11, tbl_12, tbl_13, tbl_14, tbl_15, tbl_16, tbl_17, tbl_18, tbl_19, tbl_20, tbl_21, tbl_22, tbl_23, tbl_24, tbl_25, tbl_26, tbl_27, tbl_28, tbl_29, tbl_30, tbl_31, W_top1, b_top1, W_top2, b_top2, W_top3):
    import jax
    import jax.numpy as jnp

    def _L0_rec_ref(x):
        import jax, jax.numpy as jnp
        import numpy as np
        NUM_FIELDS = 32
        n = x.shape[1]
        gram = jnp.einsum('bnd,bmd->bnm', x, x)
        rows, cols = jnp.triu_indices(n, k=1)
        inner_product = gram[:, rows, cols][..., None]
        return inner_product
    e = jnp.stack([tbl_0[ids[:, 0]], tbl_1[ids[:, 1]], tbl_2[ids[:, 2]], tbl_3[ids[:, 3]], tbl_4[ids[:, 4]], tbl_5[ids[:, 5]], tbl_6[ids[:, 6]], tbl_7[ids[:, 7]], tbl_8[ids[:, 8]], tbl_9[ids[:, 9]], tbl_10[ids[:, 10]], tbl_11[ids[:, 11]], tbl_12[ids[:, 12]], tbl_13[ids[:, 13]], tbl_14[ids[:, 14]], tbl_15[ids[:, 15]], tbl_16[ids[:, 16]], tbl_17[ids[:, 17]], tbl_18[ids[:, 18]], tbl_19[ids[:, 19]], tbl_20[ids[:, 20]], tbl_21[ids[:, 21]], tbl_22[ids[:, 22]], tbl_23[ids[:, 23]], tbl_24[ids[:, 24]], tbl_25[ids[:, 25]], tbl_26[ids[:, 26]], tbl_27[ids[:, 27]], tbl_28[ids[:, 28]], tbl_29[ids[:, 29]], tbl_30[ids[:, 30]], tbl_31[ids[:, 31]]], axis=1)
    z = _L0_rec_ref(e)
    z = z.reshape(z.shape[0], -1)
    h = jnp.concatenate([z, dense_ctx], axis=1)
    h = jnp.maximum(h @ W_top1 + b_top1, 0.0)
    h = jnp.maximum(h @ W_top2 + b_top2, 0.0)
    y = h @ W_top3
    return y

_drawn_inputs = setup_inputs


def setup_inputs(seed=0):
    import zlib

    import numpy as np

    out = dict(_drawn_inputs(seed))
    spreads = {'b_top1': (0.0, 0.1), 'b_top2': (0.0, 0.1)}
    factors = {}
    for name, (base, spread) in spreads.items():
        noise = np.random.default_rng([zlib.crc32(name.encode()), seed]).standard_normal(out[name].shape)
        drawn = base * np.exp(spread * noise) if base else spread * noise
        out[name] = jnp.asarray(drawn.astype(out[name].dtype))
    for name, factor in factors.items():
        out[name] = (out[name] * factor).astype(out[name].dtype)
    return out
```

```python
from contextlib import ExitStack

import numpy as np

import concourse.bass as bass
from concourse import mybir

BATCH, FIELDS, DIM, DENSE = 2048, 32, 64, 16
HIDDEN1, HIDDEN2 = 512, 256
P = 128
TILES = 2
SUPER = TILES * P
SUPERS = BATCH // SUPER
HALF = FIELDS // 2
QUAD = P // FIELDS
QUADS = SUPER // QUAD
BATCH_Q = 8
GRAM_BATCHES = QUADS // BATCH_Q
GROUP_F = 4
GROUPS = FIELDS // GROUP_F
CHUNKS = HALF // QUAD
OT1, OT2 = HIDDEN1 // P, HIDDEN2 // P
EMPTY = 2 * GROUPS // 2
GRAM_EMPTY = 2


def slot_meaning():
    pair = {}
    for a in range(FIELDS):
        for b in range(a + 1, FIELDS):
            pair[a, b] = len(pair)
    rows = np.zeros((P, CHUNKS), np.int64)
    second = np.zeros((FIELDS, HALF), np.int32)
    for n in range(FIELDS):
        for j in range(HALF):
            second[n, j] = j <= n if n < HALF else n - HALF < j
            other = HALF + j if second[n, j] else j
            if n == HALF + j:
                row = len(pair) + j
            else:
                row = pair[min(n, other), max(n, other)]
            rows[(j // CHUNKS) * FIELDS + n, j % CHUNKS] = row
    assert sorted(rows.ravel()) == list(range(HIDDEN1))
    return rows, np.tile(second, (QUAD, 1))


def build(nc, ids, tables, dense, w1, b1, w2, b2, w3, identity, second, out):
    fp32, i32 = mybir.dt.float32, mybir.dt.int32
    ALU, ACT = mybir.AluOpType, mybir.ActivationFunctionType
    ids_v = ids.rearrange("(s t p) f -> s p t f", t=TILES, p=P)

    ctx = ExitStack()
    with ctx:
        def sb(name, shape, dt):
            return ctx.enter_context(nc.sbuf_tensor(name, shape, dt))

        def ps(name, shape, dt):
            return ctx.enter_context(nc.psum_tensor(name, shape, dt))

        def sem(name):
            return ctx.enter_context(nc.semaphore(name))

        index = sb("index", [P, 2, TILES, FIELDS], i32)
        rows = sb("rows", [P, 2, FIELDS, TILES, DIM], fp32)
        emb_t = sb("emb_t", [P, P, FIELDS], fp32)
        folded = sb("folded", [P, QUAD, HALF, QUADS], fp32)
        pairs = sb("pairs", [P, QUAD, CHUNKS, QUADS], fp32)
        h1 = sb("h1", [P, OT1, SUPER], fp32)
        h2 = sb("h2", [P, OT2, SUPER], fp32)
        y = sb("y", [1, BATCH], fp32)
        w1_sb = sb("w1_sb", [P, CHUNKS, HIDDEN1], fp32)
        w2_sb = sb("w2_sb", [P, OT1, HIDDEN2], fp32)
        w3_sb = sb("w3_sb", [P, OT2], fp32)
        b1_sb = sb("b1_sb", [P, OT1], fp32)
        b2_sb = sb("b2_sb", [P, OT2], fp32)
        ident_sb = sb("ident_sb", [P, P], fp32)
        second_sb = sb("second_sb", [P, HALF], i32)
        turn_ps = ps("turn_ps", [P, 2, GROUP_F, P], fp32)
        gram_ps = ps("gram_ps", [P, 2, BATCH_Q, QUAD, 2, HALF], fp32)
        mlp_ps = ps("mlp_ps", [P, 2, 2, SUPER], fp32)

        index_loaded = [sem("index_loaded_even"), sem("index_loaded_odd")]
        rows_landed = [[sem(f"rows_landed_{p}_{g}") for g in range(GROUPS)] for p in range(2)]
        weights_loaded = sem("weights_loaded")
        ident_loaded = sem("ident_loaded")
        second_loaded = sem("second_loaded")
        turned = sem("turned")
        turned_by_act = sem("turned_by_act")
        turned_by_dve = sem("turned_by_dve")
        gram_ready = sem("gram_ready")
        first_copied = sem("first_copied")
        second_copied = sem("second_copied")
        pairs_moved = sem("pairs_moved")
        dense_placed = sem("dense_placed")
        layer1_ready = sem("layer1_ready")
        h1_ready = sem("h1_ready")
        layer2_ready = sem("layer2_ready")
        h2_ready = sem("h2_ready")
        layer3_ready = sem("layer3_ready")
        y_ready = sem("y_ready")
        y_stored = sem("y_stored")
        gathers_begun = sem("gathers_begun")
        folds_begun = sem("folds_begun")
        block = ctx.enter_context(nc.Block())

        ids_v = ids.rearrange("(s t p) f -> s p t f", t=TILES, p=P)
        WEIGHTS = 5

        @block.sync
        def _(sp):
            sp.dma_start(index[:, 0], ids_v[0]).then_inc(index_loaded[0], 16)
            sp.dma_start(index[:, 1], ids_v[1]).then_inc(index_loaded[1], 16)
            sp.dma_start(ident_sb[:], identity).then_inc(ident_loaded, 16)
            sp.dma_start(second_sb[:], second).then_inc(second_loaded, 16)
            for to, of in ((w1_sb, w1), (b1_sb, b1), (w2_sb, w2), (b2_sb, b2), (w3_sb, w3)):
                sp.dma_start(to[:], of).then_inc(weights_loaded, 16)

            def rearrange_pairs(s):
                sp.wait_ge(second_copied, GRAM_EMPTY + GRAM_BATCHES * (s + 1))
                for i in range(QUAD):
                    for jq in range(QUAD):
                        sp.dma_start(pairs[FIELDS * jq:FIELDS * (jq + 1), i],
                                     folded[FIELDS * i:FIELDS * (i + 1), i, CHUNKS * jq:CHUNKS * (jq + 1), :]
                                     ).then_inc(pairs_moved, 16)
                sp.wait_ge(pairs_moved, 16 * QUAD * QUAD * (s + 1))
                for jj in range(CHUNKS):
                    sp.dma_start(pairs[HALF + jj:P:FIELDS + CHUNKS, :, jj, :],
                                 dense[s].rearrange("(a b) (i q) -> b a i q", b=CHUNKS, i=QUAD)[jj]
                                 ).then_inc(dense_placed, 16)

            def refill_index(s, parity):
                sp.dma_start(index[:, parity], ids_v[s]).then_inc(index_loaded[parity], 16)

            with sp.Fori(0, SUPERS // 2 - 1) as pair:
                rearrange_pairs(2 * pair)
                refill_index(2 * pair + 2, 0)
                rearrange_pairs(2 * pair + 1)
                refill_index(2 * pair + 3, 1)
            rearrange_pairs(SUPERS - 2)
            rearrange_pairs(SUPERS - 1)
            sp.wait_ge(y_ready, 1 + SUPERS)
            sp.dma_start(out.rearrange("b o -> o b"), y[:]).then_inc(y_stored, 16)
            sp.wait_ge(y_stored, 16)

        @block.gpsimd
        def _(pool):
            def gather(s, parity, turn):
                pool.wait_ge(index_loaded[parity], 16 * (turn + 1))
                pool.wait_ge(turned_by_act, EMPTY + GROUPS // 2 * (s - 1))
                pool.wait_ge(turned_by_dve, EMPTY + GROUPS // 2 * (s - 1))
                pool.sem_inc(gathers_begun, 1)
                for f in range(FIELDS):
                    for t in range(TILES):
                        nc.gpsimd.indirect_dma_start(
                            rows[:, parity, f, t, :], None, tables[f][:, :],
                            bass.IndirectOffsetOnAxis(index[:, parity, t, f:f + 1], 0),
                        ).then_inc(rows_landed[parity][f // GROUP_F], 16)

            with pool.Fori(0, SUPERS // 2) as pair:
                gather(2 * pair, 0, pair)
                gather(2 * pair + 1, 1, pair)

        @block.tensor
        def _(pe):
            def transpose_group(s, parity, turn, g):
                pe.wait_ge(rows_landed[parity][g], 16 * TILES * GROUP_F * (turn + 1))
                n = GROUPS // 2 * s + g // 2
                pe.wait_ge((turned_by_act, turned_by_dve)[g % 2], EMPTY + n)
                for k in range(GROUP_F):
                    last = nc.tensor.transpose(turn_ps[:, g % 2, k, :],
                                               rows[:, parity, GROUP_F * g + k].rearrange("p t d -> p (t d)"), ident_sb[:])
                last.then_inc(turned, 1)

            def gram_batch(s, k):
                pe.wait_ge(second_copied, GRAM_EMPTY + GRAM_BATCHES * s + k - 1)
                for u in range(BATCH_Q):
                    quad = BATCH_Q * k + u
                    t, q = quad // (QUADS // TILES), quad % (QUADS // TILES)
                    e = emb_t[DIM * t:DIM * (t + 1), QUAD * q:QUAD * (q + 1), :].rearrange("p b f -> p (b f)")
                    last = nc.tensor.matmul(gram_ps[:, k % 2, u].rearrange("p i h j -> p (i h j)"), e, e,
                                            start=True, stop=True)
                last.then_inc(gram_ready, 1)

            def layer1_tile(s, o):
                if o == 0:
                    pe.wait_ge(dense_placed, 16 * CHUNKS * (s + 1))
                if o == OT1 // 2:
                    pe.wait_ge(y_ready, s + 1)
                for jj in range(CHUNKS):
                    last = nc.tensor.matmul(mlp_ps[:, o // 2, o % 2, :], w1_sb[:, jj, P * o:P * (o + 1)],
                                            pairs[:, :, jj, :], start=(jj == 0), stop=(jj == CHUNKS - 1))
                if o % 2:
                    last.then_inc(layer1_ready, 1)

            def layer2(s):
                pe.wait_ge(h1_ready, OT1 * (s + 1))
                for o in range(OT2):
                    for k in range(OT1):
                        last = nc.tensor.matmul(mlp_ps[:, 0, o, :], w2_sb[:, k, P * o:P * (o + 1)], h1[:, k, :],
                                                start=(k == 0), stop=(k == OT1 - 1))
                last.then_inc(layer2_ready, 1)

            def layer3(s):
                pe.wait_ge(h2_ready, OT2 * (s + 1))
                for k in range(OT2):
                    last = nc.tensor.matmul(mlp_ps[0:1, 1, 0, :], w3_sb[:, k:k + 1], h2[:, k, :],
                                            start=(k == 0), stop=(k == OT2 - 1))
                last.then_inc(layer3_ready, 1)

            def step(s, parity, turn, mlp=True):
                for o in range(OT1):
                    transpose_group(s, parity, turn, 2 * o)
                    transpose_group(s, parity, turn, 2 * o + 1)
                    if mlp:
                        layer1_tile(s - 1, o)
                pe.wait_ge(turned_by_act, EMPTY + GROUPS // 2 * (s + 1))
                pe.wait_ge(turned_by_dve, EMPTY + GROUPS // 2 * (s + 1))
                for k in range(GRAM_BATCHES):
                    gram_batch(s, k)
                    if mlp and k == 1:
                        layer2(s - 1)
                    if mlp and k == 3:
                        layer3(s - 1)

            pe.wait_ge(ident_loaded, 16)
            step(0, 0, 0, mlp=False)
            pe.wait_ge(weights_loaded, 16 * WEIGHTS)
            with pe.Fori(0, SUPERS // 2 - 1) as pair:
                step(2 * pair + 1, 1, pair)
                step(2 * pair + 2, 0, pair + 1)
            step(SUPERS - 1, 1, SUPERS // 2 - 1)
            for o in range(OT1):
                layer1_tile(SUPERS - 1, o)
            layer2(SUPERS - 1)
            layer3(SUPERS - 1)

        def drain_turned(engine, copy, done, s, g):
            engine.wait_ge(turned, GROUPS * s + g + 1)
            copy(emb_t[:, :, GROUP_F * g:GROUP_F * (g + 1)].rearrange("p b f -> p f b"),
                 turn_ps[:, g % 2]).then_inc(done, 1)

        @block.scalar
        def _(act):
            act.sem_inc(turned_by_act, EMPTY)

            def layer1_half(s, half):
                act.wait_ge(layer1_ready, 2 * s + half + 1)
                for o in (2 * half, 2 * half + 1):
                    nc.scalar.activation(h1[:, o, :], mlp_ps[:, half, o % 2, :], ACT.Relu,
                                         bias=b1_sb[:, o:o + 1]).then_inc(h1_ready, 1)

            def step(s, mlp=True):
                for half in range(2):
                    for g in (4 * half, 4 * half + 2):
                        drain_turned(act, nc.scalar.copy, turned_by_act, s, g)
                    if mlp:
                        layer1_half(s - 1, half)
                for k in range(GRAM_BATCHES):
                    act.wait_ge(gram_ready, GRAM_BATCHES * s + k + 1)
                    nc.scalar.copy(folded[:, :, :, BATCH_Q * k:BATCH_Q * (k + 1)].rearrange("p i j q -> p q i j"),
                                   gram_ps[:, k % 2, :, :, 0, :]).then_inc(first_copied, 1)

            step(0, mlp=False)
            act.wait_ge(weights_loaded, 16 * WEIGHTS)
            with act.Fori(0, SUPERS // 2 - 1) as pair:
                step(2 * pair + 1)
                step(2 * pair + 2)
            step(SUPERS - 1)
            layer1_half(SUPERS - 1, 0)
            layer1_half(SUPERS - 1, 1)

        @block.vector
        def _(dve):
            dve.sem_inc(turned_by_dve, EMPTY)
            dve.sem_inc(second_copied, GRAM_EMPTY)
            dve.sem_inc(y_ready, 1)

            def layer2_drain(s):
                dve.wait_ge(layer2_ready, s + 1)
                for o in range(OT2):
                    nc.vector.tensor_scalar(h2[:, o, :], mlp_ps[:, 0, o, :], b2_sb[:, o:o + 1], 0.0,
                                            ALU.add, ALU.max).then_inc(h2_ready, 1)

            def layer3_drain(s):
                dve.wait_ge(layer3_ready, s + 1)
                nc.vector.tensor_copy(y[:, bass.ds(s * SUPER, SUPER)].rearrange("o (q i) -> o i q", i=QUAD),
                                      mlp_ps[0:1, 1, 0, :].rearrange("o (i q) -> o i q", i=QUAD)).then_inc(y_ready, 1)

            def step(s, mlp=True):
                for g in range(1, GROUPS, 2):
                    drain_turned(dve, nc.vector.tensor_copy, turned_by_dve, s, g)
                for k in range(GRAM_BATCHES):
                    dve.wait_ge(first_copied, GRAM_BATCHES * s + k + 1)
                    dve.sem_inc(folds_begun, 1)
                    nc.vector.copy_predicated(
                        folded[:, :, :, BATCH_Q * k:BATCH_Q * (k + 1)].rearrange("p i j q -> p q i j"),
                        second_sb[:].unsqueeze(1).unsqueeze(1).to_broadcast([P, BATCH_Q, QUAD, HALF]),
                        gram_ps[:, k % 2, :, :, 1, :]).then_inc(second_copied, 1)
                    if mlp and k == 2:
                        layer2_drain(s - 1)
                    if mlp and k == 4:
                        layer3_drain(s - 1)

            dve.wait_ge(second_loaded, 16)
            step(0, mlp=False)
            dve.wait_ge(weights_loaded, 16 * WEIGHTS)
            with dve.Fori(0, SUPERS // 2 - 1) as pair:
                step(2 * pair + 1)
                step(2 * pair + 2)
            step(SUPERS - 1)
            layer2_drain(SUPERS - 1)
            layer3_drain(SUPERS - 1)


def kernel(**inputs):
    import concourse.bacc as bacc
    from concourse.bass_utils import run_bass_kernel_spmd

    nc = bacc.Bacc("TRN2", target_bir_lowering=False, num_devices=1)
    arrays = {}

    def given(name, a):
        a = np.ascontiguousarray(a)
        arrays[name] = a
        return nc.dram_tensor(name, a.shape, mybir.dt.from_np(a.dtype), kind="ExternalInput").ap()

    rows, second = slot_meaning()
    x = {k: np.asarray(v) for k, v in inputs.items()}
    ids = given("ids", x["ids"])
    tables = [given(f"tbl_{f}", x[f"tbl_{f}"]) for f in range(FIELDS)]
    dense = given("dense", x["dense_ctx"].reshape(SUPERS, SUPER // QUAD, QUAD, DENSE).transpose(0, 3, 2, 1)
                  .reshape(SUPERS, DENSE, SUPER))
    w1 = given("w1", x["W_top1"][rows])
    b1 = given("b1", x["b_top1"].reshape(OT1, P).T)
    w2 = given("w2", x["W_top2"].reshape(OT1, P, HIDDEN2).transpose(1, 0, 2))
    b2 = given("b2", x["b_top2"].reshape(OT2, P).T)
    w3 = given("w3", x["W_top3"].reshape(OT2, P).T)
    identity = given("identity", np.eye(P, dtype=np.float32))
    second = given("second", second)
    out = nc.dram_tensor("out", (BATCH, 1), mybir.dt.float32, kind="ExternalOutput").ap()
    build(nc, ids, tables, dense, w1, b1, w2, b2, w3, identity, second, out)
    return run_bass_kernel_spmd(nc, [arrays], core_ids=[0]).results[0]["out"]
```

```python
from contextlib import ExitStack

import numpy as np

import concourse.bass as bass
from concourse import mybir

BATCH, FIELDS, DIM, DENSE = 2048, 32, 64, 16
HIDDEN1, HIDDEN2 = 512, 256
P = 128
TILES = 2
SUPER = TILES * P
SUPERS = BATCH // SUPER
HALF = FIELDS // 2
QUAD = P // FIELDS
QUADS = SUPER // QUAD
BATCH_Q = 8
GRAM_BATCHES = QUADS // BATCH_Q
GROUP_F = 4
GROUPS = FIELDS // GROUP_F
CHUNKS = HALF // QUAD
OT1, OT2 = HIDDEN1 // P, HIDDEN2 // P
VOCAB = [12500, 12500, 12500, 1250, 12500, 12500, 12500, 125000, 12500, 1250, 1000, 1000, 1250, 1000, 1250, 1250,
         1250, 12500, 1000, 12500, 12500, 125000, 1000, 1250, 1000, 1250, 1000, 1000, 12500, 12500, 1000, 12500]
LOOKED_UP = sorted(range(FIELDS), key=lambda f: (VOCAB[f], f))[:12]
GATHERED = [f for f in range(FIELDS) if f not in LOOKED_UP]
SLOT_FIELD = LOOKED_UP + GATHERED
UNITS = len(LOOKED_UP)
LOOKED_GROUPS = UNITS // GROUP_F
TP = 125
SPAN = [VOCAB[f] // TP for f in LOOKED_UP]
SPAN_MAX = max(SPAN)
SPAN_AT = [sum(SPAN[:u]) for u in range(UNITS + 1)]
PARTS = 3
RING = 4
PIECES = 4
PIECE = UNITS // PIECES
UNITS_BEFORE = [(UNITS * k // GRAM_BATCHES, UNITS * (k + 1) // GRAM_BATCHES) for k in range(GRAM_BATCHES)][::-1]
UNITS_BEFORE = [(UNITS - b, UNITS - a) for a, b in UNITS_BEFORE]
LAYER1_BEFORE, LAYER2_BEFORE, LAYER3_BEFORE = (4, 5), 6, 7
EMPTY = 2 * GROUPS // 2
GRAM_EMPTY = 2


def slot_meaning():
    pair = {}
    for a in range(FIELDS):
        for b in range(a + 1, FIELDS):
            pair[a, b] = len(pair)
    rows = np.zeros((P, CHUNKS), np.int64)
    second = np.zeros((FIELDS, HALF), np.int32)
    for n in range(FIELDS):
        for j in range(HALF):
            second[n, j] = j <= n if n < HALF else n - HALF < j
            other = HALF + j if second[n, j] else j
            if n == HALF + j:
                row = len(pair) + j
            else:
                row = pair[tuple(sorted((SLOT_FIELD[n], SLOT_FIELD[other])))]
            rows[(j // CHUNKS) * FIELDS + n, j % CHUNKS] = row
    assert sorted(rows.ravel()) == list(range(HIDDEN1))
    return rows, np.tile(second, (QUAD, QUAD))


def build(nc, ids, tables, dense, w1, b1, w2, b2, w3, identity, second, looked_ids, row_numbers, out):
    fp32, i32, bf16, fp16 = mybir.dt.float32, mybir.dt.int32, mybir.dt.bfloat16, mybir.dt.float16
    ALU, ACT, AX = mybir.AluOpType, mybir.ActivationFunctionType, mybir.AxisListType
    ids_v = ids.rearrange("(s t p) f -> s p t f", t=TILES, p=P)

    ctx = ExitStack()
    with ctx:
        def sb(name, shape, dt):
            return ctx.enter_context(nc.sbuf_tensor(name, shape, dt))

        def ps(name, shape, dt):
            return ctx.enter_context(nc.psum_tensor(name, shape, dt))

        def sem(name):
            return ctx.enter_context(nc.semaphore(name))

        index = sb("index", [P, 2, TILES, FIELDS], i32)
        rows = sb("rows", [P, 2, FIELDS, TILES, DIM], fp32)
        emb_t = sb("emb_t", [P, P, FIELDS], fp32)
        folded = sb("folded", [P, 2, QUAD, HALF, QUADS], fp32)
        pairs = sb("pairs", [P, QUAD, CHUNKS, QUADS], fp32)
        h1 = sb("h1", [P, OT1, SUPER], fp32)
        h2 = sb("h2", [P, OT2, SUPER], fp32)
        y = sb("y", [1, BATCH], fp32)
        w1_sb = sb("w1_sb", [P, CHUNKS, HIDDEN1], fp32)
        w2_sb = sb("w2_sb", [P, OT1, HIDDEN2], fp32)
        w3_sb = sb("w3_sb", [P, OT2], fp32)
        b1_sb = sb("b1_sb", [P, OT1], fp32)
        b2_sb = sb("b2_sb", [P, OT2], fp32)
        ident_sb = sb("ident_sb", [P, P], fp32)
        second_sb = sb("second_sb", [P, QUAD * HALF], i32)
        split_sb = sb("split_sb", [TP, SPAN_AT[-1], PARTS, DIM], bf16)
        row_sb = sb("row_sb", [TP, SPAN_AT[-1]], fp32)
        ids32 = sb("ids32", [TP, UNITS, SUPER], i32)
        ids16 = sb("ids16", [TP, UNITS, SUPER], fp16)
        onehot = sb("onehot", [TP, RING, SPAN_MAX, SUPER], bf16)
        spare = [emb_t[0:TP].rearrange("p b f -> p (b f)"), folded[0:TP, 1].rearrange("p i j q -> p (i j q)")]
        per_spare = UNITS // 2
        whole = [spare[u // per_spare][:, (SPAN_AT[u] - SPAN_AT[u - u % per_spare]) * DIM:
                                       (SPAN_AT[u + 1] - SPAN_AT[u - u % per_spare]) * DIM] for u in range(UNITS)]
        residue = [h1[0:TP].rearrange("p o b -> p (o b)"), pairs[0:TP].rearrange("p i j q -> p (i j q)")]
        turn_ps = ps("turn_ps", [P, 2, GROUP_F, P], fp32)
        gram_ps = ps("gram_ps", [P, 2, TILES, BATCH_Q // TILES, 2, QUAD * HALF], fp32)
        mlp_ps = ps("mlp_ps", [P, 2, 2, SUPER], fp32)
        turn_bank = [turn_ps[:, 0], turn_ps[:, 1]] + [
            mlp_ps[:, h].rearrange("p a b -> p (a b)").rearrange("p (k b) -> p k b", k=GROUP_F) for h in range(2)]

        index_loaded = [sem("index_loaded_even"), sem("index_loaded_odd")]
        rows_landed = [[sem(f"rows_landed_{p}_{g}") for g in range(GROUPS)] for p in range(2)]
        weights_loaded = sem("weights_loaded")
        ident_loaded = sem("ident_loaded")
        second_loaded = sem("second_loaded")
        turned = sem("turned")
        turned_by_act = sem("turned_by_act")
        turned_by_dve = sem("turned_by_dve")
        gram_ready = sem("gram_ready")
        first_copied = sem("first_copied")
        second_copied = sem("second_copied")
        pairs_moved = sem("pairs_moved")
        dense_placed = sem("dense_placed")
        layer1_ready = sem("layer1_ready")
        h1_ready = sem("h1_ready")
        layer2_ready = sem("layer2_ready")
        h2_ready = sem("h2_ready")
        layer3_ready = sem("layer3_ready")
        y_ready = sem("y_ready")
        y_stored = sem("y_stored")
        whole_loaded = [sem(f"whole_loaded_{u}") for u in range(UNITS)]
        row_loaded = sem("row_loaded")
        ids32_loaded = sem("ids32_loaded")
        ids_converted = sem("ids_converted")
        high_split = sem("high_split")
        high_taken = sem("high_taken")
        middle_split = sem("middle_split")
        table_split = sem("table_split")
        onehot_ready = sem("onehot_ready")
        lookup_ready = sem("lookup_ready")
        looked_up = sem("looked_up")
        gathers_begun = sem("gathers_begun")
        folds_begun = sem("folds_begun")
        block = ctx.enter_context(nc.Block())

        ids_v = ids.rearrange("(s t p) f -> s p t f", t=TILES, p=P)
        WEIGHTS = 5

        @block.sync
        def _(sp):
            sp.dma_start(index[:, 0], ids_v[0]).then_inc(index_loaded[0], 16)
            sp.dma_start(index[:, 1], ids_v[1]).then_inc(index_loaded[1], 16)
            sp.dma_start(ids32[:], looked_ids[0:1].to_broadcast([TP, UNITS, SUPER])).then_inc(ids32_loaded, 16)
            sp.dma_start(row_sb[:], row_numbers).then_inc(row_loaded, 16)
            for u, f in enumerate(LOOKED_UP):
                sp.dma_start(whole[u], tables[f].rearrange("(p c) d -> p (c d)", p=TP)).then_inc(whole_loaded[u], 16)
            sp.dma_start(ident_sb[:], identity).then_inc(ident_loaded, 16)
            sp.dma_start(second_sb[:], second).then_inc(second_loaded, 16)
            for to, of in ((w1_sb, w1), (b1_sb, b1), (w2_sb, w2), (b2_sb, b2), (w3_sb, w3)):
                sp.dma_start(to[:], of).then_inc(weights_loaded, 16)

            def rearrange_pairs(s, parity):
                sp.wait_ge(second_copied, GRAM_EMPTY + GRAM_BATCHES * (s + 1))
                for i in range(QUAD):
                    for jq in range(QUAD):
                        sp.dma_start(pairs[FIELDS * jq:FIELDS * (jq + 1), i],
                                     folded[FIELDS * i:FIELDS * (i + 1), parity, i, CHUNKS * jq:CHUNKS * (jq + 1), :]
                                     ).then_inc(pairs_moved, 16)
                sp.wait_ge(pairs_moved, 16 * QUAD * QUAD * (s + 1))
                for jj in range(CHUNKS):
                    sp.dma_start(pairs[HALF + jj:P:FIELDS + CHUNKS, :, jj, :],
                                 dense[s].rearrange("(a b) (i q) -> b a i q", b=CHUNKS, i=QUAD)[jj]
                                 ).then_inc(dense_placed, 16)

            def refill_index(s, parity):
                sp.wait_ge(turned, GROUPS * (s - 1))
                sp.dma_start(index[:, parity], ids_v[s]).then_inc(index_loaded[parity], 16)

            def refill_ids32(s):
                sp.wait_ge(ids_converted, PIECES * s)
                sp.dma_start(ids32[:], looked_ids[bass.ds(s, 1)].to_broadcast([TP, UNITS, SUPER])
                             ).then_inc(ids32_loaded, 16)

            refill_ids32(1)
            with sp.Fori(0, SUPERS // 2 - 1) as pair:
                refill_index(2 * pair + 2, 0)
                refill_ids32(2 * pair + 2)
                rearrange_pairs(2 * pair, 0)
                refill_index(2 * pair + 3, 1)
                refill_ids32(2 * pair + 3)
                rearrange_pairs(2 * pair + 1, 1)
            rearrange_pairs(SUPERS - 2, 0)
            rearrange_pairs(SUPERS - 1, 1)
            sp.wait_ge(y_ready, 1 + SUPERS)
            sp.dma_start(out.rearrange("b o -> o b"), y[:]).then_inc(y_stored, 16)
            sp.wait_ge(y_stored, 16)

        @block.gpsimd
        def _(pool):
            def gather(s, parity, turn):
                pool.wait_ge(index_loaded[parity], 16 * (turn + 1))
                pool.wait_ge(turned_by_act, EMPTY + GROUPS // 2 * (s - 1))
                pool.wait_ge(turned_by_dve, EMPTY + GROUPS // 2 * (s - 1))
                pool.sem_inc(gathers_begun, 1)
                for slot in range(UNITS, FIELDS):
                    f = SLOT_FIELD[slot]
                    for t in range(TILES):
                        nc.gpsimd.indirect_dma_start(
                            rows[:, parity, slot, t, :], None, tables[f][:, :],
                            bass.IndirectOffsetOnAxis(index[:, parity, t, f:f + 1], 0),
                        ).then_inc(rows_landed[parity][slot // GROUP_F], 16)

            with pool.Fori(0, SUPERS // 2) as pair:
                gather(2 * pair, 0, pair)
                gather(2 * pair + 1, 1, pair)

        @block.tensor
        def _(pe):
            def transpose_group(s, parity, turn, g, mlp):
                if g == 0:
                    pe.wait_ge(looked_up, UNITS * (s + 1))
                if g >= LOOKED_GROUPS:
                    pe.wait_ge(rows_landed[parity][g], 16 * TILES * GROUP_F * (turn + 1))
                if g == 3 and mlp:
                    pe.wait_ge(y_ready, s)
                if g >= 4:
                    pe.wait_ge((turned_by_act, turned_by_dve)[g % 2],
                               EMPTY + GROUPS // 2 * s + g // 2 - 1)
                for k in range(GROUP_F):
                    last = nc.tensor.transpose(turn_bank[g % 4][:, k, :],
                                               rows[:, parity, GROUP_F * g + k].rearrange("p t d -> p (t d)"), ident_sb[:])
                last.then_inc(turned, 1)

            def look_up(s, u, first=False):
                n = UNITS * s + u
                if first:
                    pe.wait_ge(table_split, u + 1)
                if u >= 2:
                    pe.wait_ge(looked_up, n - 1)
                elif not first:
                    pe.wait_ge((turned_by_act, turned_by_dve)[u], EMPTY + GROUPS // 2 * s - 1)
                pe.wait_ge(onehot_ready, n + 1)
                for t in range(TILES):
                    for c in range(SPAN[u]):
                        last = nc.tensor.matmul(
                            turn_ps[:, u % 2].rearrange("p k b -> p (k b)")[:, t * PARTS * DIM:(t + 1) * PARTS * DIM],
                            onehot[:, u % RING, c, P * t:P * (t + 1)],
                            split_sb[:, SPAN_AT[u] + c].rearrange("p a d -> p (a d)"),
                            start=(c == 0), stop=(c == SPAN[u] - 1))
                last.then_inc(lookup_ready, 1)

            def gram_batch(s, k):
                pe.wait_ge(second_copied, GRAM_EMPTY + GRAM_BATCHES * s + k - 1)
                for u in range(BATCH_Q):
                    quad = BATCH_Q * k + u
                    t, q = u % TILES, (BATCH_Q * k + u) // TILES
                    e = emb_t[DIM * t:DIM * (t + 1), QUAD * q:QUAD * (q + 1), :]
                    last = nc.tensor.matmul(gram_ps[:, k % 2, t, u // TILES].rearrange("p h ij -> p (h ij)"),
                                            e.rearrange("p b f -> p (b f)"),
                                            e.rearrange("p b (h j) -> p h b j", h=2),
                                            start=True, stop=True)
                last.then_inc(gram_ready, 1)

            def layer1_tile(s, o):
                if o == 0:
                    pe.wait_ge(dense_placed, 16 * CHUNKS * (s + 1))
                if o == OT1 // 2:
                    pe.wait_ge(y_ready, s + 1)
                for jj in range(CHUNKS):
                    last = nc.tensor.matmul(mlp_ps[:, o // 2, o % 2, :], w1_sb[:, jj, P * o:P * (o + 1)],
                                            pairs[:, :, jj, :], start=(jj == 0), stop=(jj == CHUNKS - 1))
                if o % 2:
                    last.then_inc(layer1_ready, 1)

            def layer2(s):
                pe.wait_ge(h1_ready, OT1 * (s + 1))
                for o in range(OT2):
                    for k in range(OT1):
                        last = nc.tensor.matmul(mlp_ps[:, 0, o, :], w2_sb[:, k, P * o:P * (o + 1)], h1[:, k, :],
                                                start=(k == 0), stop=(k == OT1 - 1))
                last.then_inc(layer2_ready, 1)

            def layer3(s):
                pe.wait_ge(h2_ready, OT2 * (s + 1))
                for k in range(OT2):
                    last = nc.tensor.matmul(mlp_ps[0:1, 1, 0, :], w3_sb[:, k:k + 1], h2[:, k, :],
                                            start=(k == 0), stop=(k == OT2 - 1))
                last.then_inc(layer3_ready, 1)

            def step(s, parity, turn, mlp=True, ahead=True):
                for g in range(GROUPS):
                    transpose_group(s, parity, turn, g, mlp)
                for k in range(GRAM_BATCHES):
                    if ahead:
                        for u in range(*UNITS_BEFORE[k]):
                            look_up(s + 1, u)
                    if k == 0:
                        pe.wait_ge(turned_by_act, EMPTY + GROUPS // 2 * (s + 1))
                        pe.wait_ge(turned_by_dve, EMPTY + GROUPS // 2 * (s + 1))
                    if mlp and k in LAYER1_BEFORE:
                        for o in range(OT1 // 2):
                            layer1_tile(s - 1, OT1 // 2 * LAYER1_BEFORE.index(k) + o)
                    if mlp and k == LAYER2_BEFORE:
                        layer2(s - 1)
                    if mlp and k == LAYER3_BEFORE:
                        layer3(s - 1)
                    gram_batch(s, k)

            for u in range(UNITS):
                look_up(0, u, first=True)
            pe.wait_ge(ident_loaded, 16)
            step(0, 0, 0, mlp=False)
            pe.wait_ge(weights_loaded, 16 * WEIGHTS)
            with pe.Fori(0, SUPERS // 2 - 1) as pair:
                step(2 * pair + 1, 1, pair)
                step(2 * pair + 2, 0, pair + 1)
            step(SUPERS - 1, 1, SUPERS // 2 - 1, ahead=False)
            for o in range(OT1):
                layer1_tile(SUPERS - 1, o)
            layer2(SUPERS - 1)
            layer3(SUPERS - 1)

        def drain_turned(engine, copy, done, s, g):
            engine.wait_ge(turned, GROUPS * s + g + 1)
            copy(emb_t[:, :, GROUP_F * g:GROUP_F * (g + 1)].rearrange("p b f -> p f b"),
                 turn_bank[g % 4]).then_inc(done, 1)

        def part(u, which):
            return split_sb[:, SPAN_AT[u]:SPAN_AT[u + 1], which, :]

        def table_rows(u, flat):
            return flat[:, 0:SPAN[u] * DIM].rearrange("p (c d) -> p c d", d=DIM)

        @block.scalar
        def _(act):
            act.sem_inc(turned_by_act, EMPTY)

            def layer1_half(s, half):
                act.wait_ge(layer1_ready, 2 * s + half + 1)
                for o in (2 * half, 2 * half + 1):
                    nc.scalar.activation(h1[:, o, :], mlp_ps[:, half, o % 2, :], ACT.Relu,
                                         bias=b1_sb[:, o:o + 1]).then_inc(h1_ready, 1)

            def convert(s, piece):
                if piece == 0:
                    act.wait_ge(ids32_loaded, 16 * (s + 1))
                us = slice(PIECE * piece, PIECE * (piece + 1))
                nc.scalar.copy(ids16[:, us, :], ids32[:, us, :]).then_inc(ids_converted, 1)

            def layer2_drain(s):
                act.wait_ge(layer2_ready, s + 1)
                for o in range(OT2):
                    nc.scalar.activation(h2[:, o, :], mlp_ps[:, 0, o, :], ACT.Relu,
                                         bias=b2_sb[:, o:o + 1]).then_inc(h2_ready, 1)

            def step(s, parity, mlp=True, ahead=True):
                for half in range(2):
                    for g in (4 * half, 4 * half + 2):
                        drain_turned(act, nc.scalar.copy, turned_by_act, s, g)
                        if ahead and half == 0:
                            convert(s + 1, g // 2)
                for k in range(GRAM_BATCHES):
                    if mlp and k in LAYER1_BEFORE:
                        layer1_half(s - 1, LAYER1_BEFORE.index(k))
                    if mlp and k == LAYER2_BEFORE:
                        layer2_drain(s - 1)
                    if ahead and k in (1, 2):
                        convert(s + 1, k + 1)
                    act.wait_ge(gram_ready, GRAM_BATCHES * s + k + 1)
                    nc.scalar.copy(folded[:, parity, :, :, BATCH_Q * k:BATCH_Q * (k + 1)].rearrange("p i j (q t) -> p t q (i j)", t=TILES),
                                   gram_ps[:, k % 2, :, :, 0, :]).then_inc(first_copied, 1)

            def high(u):
                act.wait_ge(whole_loaded[u], 16)
                nc.scalar.copy(part(u, 0), table_rows(u, whole[u])).then_inc(high_split, 1)

            def middle(u):
                act.wait_ge(high_taken, u + 1)
                nc.scalar.copy(part(u, 1), table_rows(u, residue[u % 2])).then_inc(middle_split, 1)

            high(0)
            for piece in range(PIECES):
                convert(0, piece)
            for u in range(UNITS):
                if u + 1 < UNITS:
                    high(u + 1)
                middle(u)
            step(0, 0, mlp=False)
            act.wait_ge(weights_loaded, 16 * WEIGHTS)
            with act.Fori(0, SUPERS // 2 - 1) as pair:
                step(2 * pair + 1, 1)
                step(2 * pair + 2, 0)
            step(SUPERS - 1, 1, ahead=False)
            layer1_half(SUPERS - 1, 0)
            layer1_half(SUPERS - 1, 1)
            layer2_drain(SUPERS - 1)

        @block.vector
        def _(dve):
            dve.sem_inc(turned_by_dve, EMPTY)
            dve.sem_inc(second_copied, GRAM_EMPTY)
            dve.sem_inc(y_ready, 1)

            def layer3_drain(s):
                dve.wait_ge(layer3_ready, s + 1)
                nc.vector.tensor_copy(y[:, bass.ds(s * SUPER, SUPER)].rearrange("o (t q i) -> o i q t", i=QUAD, t=TILES),
                                      mlp_ps[0:1, 1, 0, :].rearrange("o (i q t) -> o i q t", i=QUAD, t=TILES)).then_inc(y_ready, 1)

            def make_onehot(s, u):
                dve.wait_ge(ids_converted, PIECES * s + u // PIECE + 1)
                for c in range(SPAN[u]):
                    last = nc.vector.tensor_scalar(onehot[:, u % RING, c, :], ids16[:, u, :],
                                                   row_sb[:, SPAN_AT[u] + c:SPAN_AT[u] + c + 1], None, ALU.is_equal)
                last.then_inc(onehot_ready, 1)

            def add_parts(s, u, parity):
                dve.wait_ge(lookup_ready, UNITS * s + u + 1)
                nc.vector.reduce_sum(
                    rows[:, parity, u, :, :],
                    turn_ps[:, u % 2].rearrange("p k b -> p (k b)")[:, 0:TILES * PARTS * DIM]
                    .rearrange("p (t a d) -> p t d a", t=TILES, a=PARTS), AX.X).then_inc(looked_up, 1)

            def step(s, parity, mlp=True, ahead=True):
                for g in range(1, GROUPS, 2):
                    drain_turned(dve, nc.vector.tensor_copy, turned_by_dve, s, g)
                    if ahead:
                        make_onehot(s + 1, g // 2)
                for k in range(GRAM_BATCHES):
                    if ahead:
                        for u in range(*UNITS_BEFORE[k]):
                            add_parts(s + 1, u, 1 - parity)
                            if u + RING < UNITS:
                                make_onehot(s + 1, u + RING)
                    if mlp and k == LAYER3_BEFORE:
                        layer3_drain(s - 1)
                    dve.wait_ge(first_copied, GRAM_BATCHES * s + k + 1)
                    dve.sem_inc(folds_begun, 1)
                    nc.vector.copy_predicated(
                        folded[:, parity, :, :, BATCH_Q * k:BATCH_Q * (k + 1)].rearrange("p i j (q t) -> p t q (i j)", t=TILES),
                        second_sb[:].unsqueeze(1).unsqueeze(1).to_broadcast([P, TILES, BATCH_Q // TILES, QUAD * HALF]),
                        gram_ps[:, k % 2, :, :, 1, :]).then_inc(second_copied, 1)

            def take_high(u):
                if u >= 2:
                    dve.wait_ge(table_split, u - 1)
                dve.wait_ge(high_split, u + 1)
                nc.vector.tensor_tensor(table_rows(u, residue[u % 2]), table_rows(u, whole[u]), part(u, 0),
                                        ALU.subtract).then_inc(high_taken, 1)

            def low(u):
                dve.wait_ge(middle_split, u + 1)
                nc.vector.tensor_tensor(part(u, 2), table_rows(u, residue[u % 2]), part(u, 1),
                                        ALU.subtract).then_inc(table_split, 1)

            dve.wait_ge(row_loaded, 16)
            take_high(0)
            for u in range(UNITS):
                if u >= RING:
                    add_parts(0, u - RING, 0)
                make_onehot(0, u)
                if u + 1 < UNITS:
                    take_high(u + 1)
                low(u)
            for u in range(UNITS - RING, UNITS):
                add_parts(0, u, 0)
            dve.wait_ge(second_loaded, 16)
            step(0, 0, mlp=False)
            with dve.Fori(0, SUPERS // 2 - 1) as pair:
                step(2 * pair + 1, 1)
                step(2 * pair + 2, 0)
            step(SUPERS - 1, 1, ahead=False)
            layer3_drain(SUPERS - 1)


def kernel(**inputs):
    import concourse.bacc as bacc
    from concourse.bass_utils import run_bass_kernel_spmd

    nc = bacc.Bacc("TRN2", target_bir_lowering=False, num_devices=1)
    arrays = {}

    def given(name, a):
        a = np.ascontiguousarray(a)
        arrays[name] = a
        return nc.dram_tensor(name, a.shape, mybir.dt.from_np(a.dtype), kind="ExternalInput").ap()

    rows, second = slot_meaning()
    x = {k: np.asarray(v) for k, v in inputs.items()}
    ids = given("ids", x["ids"])
    tables = [given(f"tbl_{f}", x[f"tbl_{f}"]) for f in range(FIELDS)]
    dense = given("dense", x["dense_ctx"].reshape(SUPERS, TILES, P // QUAD, QUAD, DENSE).transpose(0, 4, 3, 2, 1)
                  .reshape(SUPERS, DENSE, SUPER))
    w1 = given("w1", x["W_top1"][rows])
    b1 = given("b1", x["b_top1"].reshape(OT1, P).T)
    w2 = given("w2", x["W_top2"].reshape(OT1, P, HIDDEN2).transpose(1, 0, 2))
    b2 = given("b2", x["b_top2"].reshape(OT2, P).T)
    w3 = given("w3", x["W_top3"].reshape(OT2, P).T)
    identity = given("identity", np.eye(P, dtype=np.float32))
    second = given("second", second)
    looked_ids = given("looked_ids", x["ids"][:, LOOKED_UP].reshape(SUPERS, SUPER, UNITS).transpose(0, 2, 1))
    row_numbers = given("row_numbers", np.concatenate(
        [np.arange(TP * n, dtype=np.float32).reshape(TP, n) for n in SPAN], axis=1))
    out = nc.dram_tensor("out", (BATCH, 1), mybir.dt.float32, kind="ExternalOutput").ap()
    build(nc, ids, tables, dense, w1, b1, w2, b2, w3, identity, second, looked_ids, row_numbers, out)
    return run_bass_kernel_spmd(nc, [arrays], core_ids=[0]).results[0]["out"]
```

```python
from contextlib import ExitStack

import numpy as np

import concourse.bass as bass
from concourse import mybir

BATCH, FIELDS, DIM, DENSE = 2048, 32, 64, 16
HIDDEN1, HIDDEN2 = 512, 256
P = 128
TILES = 2
SUPER = TILES * P
SUPERS = BATCH // SUPER
HALF = FIELDS // 2
QUAD = P // FIELDS
QUADS = SUPER // QUAD
WARM_BEFORE, WARM_AFTER = 32, 10
BATCH_Q = 8
GRAM_BATCHES = QUADS // BATCH_Q
GROUP_F = 4
GROUPS = FIELDS // GROUP_F
CHUNKS = HALF // QUAD
OT1, OT2 = HIDDEN1 // P, HIDDEN2 // P
VOCAB = [12500, 12500, 12500, 1250, 12500, 12500, 12500, 125000, 12500, 1250, 1000, 1000, 1250, 1000, 1250, 1250,
         1250, 12500, 1000, 12500, 12500, 125000, 1000, 1250, 1000, 1250, 1000, 1000, 12500, 12500, 1000, 12500]
LOOKED_UP = sorted(range(FIELDS), key=lambda f: (VOCAB[f], f))[:11]
GATHERED = [f for f in range(FIELDS) if f not in LOOKED_UP]
SLOT_FIELD = LOOKED_UP + GATHERED
UNITS = len(LOOKED_UP)
GATHERS_IN = [sum(slot >= UNITS for slot in range(g * GROUP_F, (g + 1) * GROUP_F)) for g in range(GROUPS)]
TP = 125
SPAN = [VOCAB[f] // TP for f in LOOKED_UP]
SPAN_MAX = max(SPAN)
assert max(VOCAB[f] for f in LOOKED_UP) < 2048
SPAN_AT = [sum(SPAN[:u]) for u in range(UNITS + 1)]
PARTS = 3
RING = 4
PIECES = [(0, 3), (3, 6), (6, 9), (9, UNITS)]
PIECE_OF = [p for p, (a, b) in enumerate(PIECES) for _ in range(a, b)]
TURN_UNITS = [[]] * 2 + [[u] for u in range(GROUPS - 2)]
GRAM_UNITS = [[u] for u in range(GROUPS - 2, UNITS)]
GRAM_UNITS += [[]] * (GRAM_BATCHES - len(GRAM_UNITS))
READY_MADE = 3
assert READY_MADE < RING and READY_MADE <= PIECES[0][1] and not any(GRAM_UNITS[GRAM_BATCHES - READY_MADE + 1:])
CONVERT_BEFORE = range(GRAM_BATCHES - len(PIECES), GRAM_BATCHES)
assert not any(GRAM_UNITS[CONVERT_BEFORE[0] + 2:])
SP_MOVES = 10
MOVES = [(i, jq) for i in range(QUAD) for jq in range(QUAD)]
LAYER1_BEFORE, LAYER2_BEFORE, LAYER3_BEFORE = (4, 5), 6, 7
EMPTY = 2 * GROUPS
GRAM_EMPTY = 2
Y_EMPTY = 2


def slot_meaning():
    pair = {}
    for a in range(FIELDS):
        for b in range(a + 1, FIELDS):
            pair[a, b] = len(pair)
    rows = np.zeros((P, CHUNKS), np.int64)
    second = np.zeros((FIELDS, HALF), np.int32)
    for n in range(FIELDS):
        for j in range(HALF):
            second[n, j] = j <= n if n < HALF else n - HALF < j
            other = HALF + j if second[n, j] else j
            if n == HALF + j:
                row = len(pair) + j
            else:
                row = pair[tuple(sorted((SLOT_FIELD[n], SLOT_FIELD[other])))]
            rows[(j // CHUNKS) * FIELDS + n, j % CHUNKS] = row
    assert sorted(rows.ravel()) == list(range(HIDDEN1))
    return rows, np.tile(second, (QUAD, QUAD))


def build(nc, ids, tables, dense, w1, b1, w2, b2, w3, identity, second, looked_ids, first_rows, out):
    fp32, i32, bf16, fp16 = mybir.dt.float32, mybir.dt.int32, mybir.dt.bfloat16, mybir.dt.float16
    ALU, ACT, AX = mybir.AluOpType, mybir.ActivationFunctionType, mybir.AxisListType
    ids_v = ids.rearrange("(s t p) f -> s p t f", t=TILES, p=P)

    ctx = ExitStack()
    with ctx:
        def sb(name, shape, dt):
            return ctx.enter_context(nc.sbuf_tensor(name, shape, dt))

        def ps(name, shape, dt):
            return ctx.enter_context(nc.psum_tensor(name, shape, dt))

        def sem(name):
            return ctx.enter_context(nc.semaphore(name))

        index = sb("index", [P, 2, TILES, FIELDS], i32)
        rows = sb("rows", [P, 2, FIELDS, TILES, DIM], fp32)
        emb_t = sb("emb_t", [P, P, FIELDS], fp32)
        folded = sb("folded", [P, 2, QUAD, HALF, QUADS], fp32)
        pairs = sb("pairs", [P, 2, QUAD, CHUNKS, QUADS], fp32)
        h1 = sb("h1", [P, OT1, SUPER], fp32)
        h2 = sb("h2", [P, OT2, SUPER], fp32)
        y = sb("y", [1, BATCH], fp32)
        w1_sb = sb("w1_sb", [P, CHUNKS, HIDDEN1], fp32)
        w2_sb = sb("w2_sb", [P, OT1, HIDDEN2], fp32)
        w3_sb = sb("w3_sb", [P, OT2], fp32)
        b1_sb = sb("b1_sb", [P, OT1], fp32)
        b2_sb = sb("b2_sb", [P, OT2], fp32)
        ident_sb = sb("ident_sb", [P, P], fp32)
        second_sb = sb("second_sb", [P, QUAD * HALF], i32)
        split_sb = sb("split_sb", [TP, SPAN_AT[-1], PARTS, DIM], bf16)
        first_sb = sb("first_sb", [TP, len(PIECES)], fp32)
        ids32 = sb("ids32", [TP, UNITS, SUPER], i32)
        place = sb("place", [TP, UNITS, SUPER], fp16)
        onehot = sb("onehot", [TP, RING, SPAN_MAX, SUPER], bf16)
        spare = [emb_t[0:TP].rearrange("p b f -> p (b f)"), folded[0:TP, 1].rearrange("p i j q -> p (i j q)")]
        per_spare = (UNITS + 1) // 2
        whole = [spare[u // per_spare][:, (SPAN_AT[u] - SPAN_AT[u - u % per_spare]) * DIM:
                                       (SPAN_AT[u + 1] - SPAN_AT[u - u % per_spare]) * DIM] for u in range(UNITS)]
        residue = [h1[0:TP].rearrange("p o b -> p (o b)"), pairs[0:TP, 0].rearrange("p i j q -> p (i j q)")]
        turn_ps = ps("turn_ps", [P, 2, GROUP_F, P], fp32)
        gram_ps = ps("gram_ps", [P, 2, TILES, BATCH_Q // TILES, 2, QUAD * HALF], fp32)
        mlp_ps = ps("mlp_ps", [P, 2, 2, SUPER], fp32)
        turn_bank = [mlp_ps[:, h].rearrange("p a b -> p (a b)").rearrange("p (k b) -> p k b", k=GROUP_F)
                     for h in range(2)] + [turn_ps[:, 0], turn_ps[:, 1]]

        index_loaded = [sem("index_loaded_even"), sem("index_loaded_odd")]
        rows_landed = [[sem(f"rows_landed_{p}_{g}") for g in range(GROUPS)] for p in range(2)]
        weights_loaded = sem("weights_loaded")
        ident_loaded = sem("ident_loaded")
        second_loaded = sem("second_loaded")
        turned = sem("turned")
        turned_drained = sem("turned_drained")
        turned_by_dve = sem("turned_by_dve")
        gram_ready = sem("gram_ready")
        first_copied = sem("first_copied")
        second_copied = sem("second_copied")
        pairs_moved = sem("pairs_moved")
        moved_by_pool = sem("moved_by_pool")
        dense_placed = [sem("dense_placed_even"), sem("dense_placed_odd")]
        layer1_ready = sem("layer1_ready")
        h1_ready = sem("h1_ready")
        layer2_ready = sem("layer2_ready")
        h2_ready = sem("h2_ready")
        layer3_ready = sem("layer3_ready")
        y_ready = sem("y_ready")
        y_stored = sem("y_stored")
        whole_loaded = [sem(f"whole_loaded_{u}") for u in range(UNITS)]
        first_loaded = sem("first_loaded")
        ids32_loaded = sem("ids32_loaded")
        ids_converted = sem("ids_converted")
        high_split = sem("high_split")
        high_taken = sem("high_taken")
        middle_split = sem("middle_split")
        table_split = sem("table_split")
        onehot_ready = sem("onehot_ready")
        lookup_ready = sem("lookup_ready")
        looked_up = sem("looked_up")
        gathers_begun = sem("gathers_begun")
        folds_begun = sem("folds_begun")
        block = ctx.enter_context(nc.Block())
        WEIGHTS = 5

        def move_cells(engine, i, jq, parity):
            return engine.dma_start(pairs[FIELDS * jq:FIELDS * (jq + 1), parity, i],
                                    folded[FIELDS * i:FIELDS * (i + 1), parity, i, CHUNKS * jq:CHUNKS * (jq + 1), :])

        @block.sync
        def _(sp):
            sp.dma_start(index[:, 0], ids_v[0]).then_inc(index_loaded[0], 16)
            sp.dma_start(index[:, 1], ids_v[1]).then_inc(index_loaded[1], 16)
            sp.dma_start(first_sb[:], first_rows).then_inc(first_loaded, 16)
            sp.dma_start(ident_sb[:], identity).then_inc(ident_loaded, 16)
            for u, f in enumerate(LOOKED_UP):
                sp.dma_start(whole[u], tables[f].rearrange("(p c) d -> p (c d)", p=TP)).then_inc(whole_loaded[u], 16)
                if u == 1:
                    sp.dma_start(ids32[:], looked_ids[0:1].to_broadcast([TP, UNITS, SUPER])).then_inc(ids32_loaded, 16)
            sp.dma_start(second_sb[:], second).then_inc(second_loaded, 16)
            for to, of in ((w1_sb, w1), (b1_sb, b1), (w2_sb, w2), (b2_sb, b2), (w3_sb, w3)):
                sp.dma_start(to[:], of).then_inc(weights_loaded, 16)

            def rearrange_pairs(s, parity, own=len(MOVES)):
                sp.wait_ge(second_copied, GRAM_EMPTY + GRAM_BATCHES * (s + 1))
                for i, jq in MOVES[:own]:
                    move_cells(sp, i, jq, parity).then_inc(pairs_moved, 16)
                sp.wait_ge(pairs_moved, 16 * (len(MOVES) * s + own))
                if own < len(MOVES):
                    sp.wait_ge(moved_by_pool, 16 * (len(MOVES) - own))
                for jj in range(CHUNKS):
                    sp.dma_start(pairs[HALF + jj:P:FIELDS + CHUNKS, parity, :, jj, :],
                                 dense[s].rearrange("(a b) (i q) -> b a i q", b=CHUNKS, i=QUAD)[jj]
                                 ).then_inc(dense_placed[parity], 16)

            def refill_index(s, parity):
                sp.wait_ge(turned, GROUPS * (s - 1))
                sp.dma_start(index[:, parity], ids_v[s]).then_inc(index_loaded[parity], 16)

            def refill_ids32(s):
                sp.wait_ge(ids_converted, len(PIECES) * s)
                sp.dma_start(ids32[:], looked_ids[bass.ds(s, 1)].to_broadcast([TP, UNITS, SUPER])
                             ).then_inc(ids32_loaded, 16)

            refill_ids32(1)
            with sp.Fori(0, SUPERS // 2 - 1) as pair:
                refill_index(2 * pair + 2, 0)
                refill_ids32(2 * pair + 2)
                rearrange_pairs(2 * pair, 0)
                refill_index(2 * pair + 3, 1)
                refill_ids32(2 * pair + 3)
                rearrange_pairs(2 * pair + 1, 1)
            refill_ids32(SUPERS)
            rearrange_pairs(SUPERS - 2, 0)
            rearrange_pairs(SUPERS - 1, 1, own=SP_MOVES)
            sp.wait_ge(y_ready, Y_EMPTY + SUPERS)
            sp.dma_start(out.rearrange("b o -> o b"), y[:]).then_inc(y_stored, 16)
            sp.wait_ge(y_stored, 16)

        @block.gpsimd
        def _(pool):
            def gather(s, parity, turn):
                pool.wait_ge(index_loaded[parity], 16 * (turn + 1))
                pool.wait_ge(turned_drained, EMPTY + GROUPS * (s - 1))
                pool.sem_inc(gathers_begun, 1)
                for slot in range(UNITS, FIELDS):
                    f = SLOT_FIELD[slot]
                    for t in range(TILES):
                        nc.gpsimd.indirect_dma_start(
                            rows[:, parity, slot, t, :], None, tables[f][:, :],
                            bass.IndirectOffsetOnAxis(index[:, parity, t, f:f + 1], 0),
                        ).then_inc(rows_landed[parity][slot // GROUP_F], 16)

            with pool.Fori(0, SUPERS // 2) as pair:
                gather(2 * pair, 0, pair)
                gather(2 * pair + 1, 1, pair)
            pool.wait_ge(second_copied, GRAM_EMPTY + GRAM_BATCHES * SUPERS)
            for i, jq in MOVES[SP_MOVES:]:
                move_cells(pool, i, jq, 1).then_inc(moved_by_pool, 16)

        @block.tensor
        def _(pe):
            def transpose_group(s, parity, turn, g, banks):
                if g == 0:
                    pe.wait_ge(looked_up, UNITS * (s + 1))
                if GATHERS_IN[g]:
                    pe.wait_ge(rows_landed[parity][g], 16 * TILES * GATHERS_IN[g] * (turn + 1))
                if g == 1:
                    pe.wait_ge(y_ready, Y_EMPTY + s - 1)
                if g >= banks and banks == 2:
                    pe.wait_ge(turned_drained, EMPTY + GROUPS * s + g - 1)
                elif g >= banks:
                    if g % 2:
                        pe.wait_ge(turned_by_dve, (g - 1) // 2 - 1)
                    else:
                        pe.wait_ge(turned_drained, EMPTY + GROUPS * s + g // 2 - 1)
                for k in range(GROUP_F):
                    last = nc.tensor.transpose(turn_bank[g % banks][:, k, :],
                                               rows[:, parity, GROUP_F * g + k].rearrange("p t d -> p (t d)"), ident_sb[:])
                last.then_inc(turned, 1)

            def look_up(s, u, first=False):
                n = UNITS * s + u
                if first:
                    pe.wait_ge(table_split, u + 1)
                if u >= 2:
                    pe.wait_ge(looked_up, n - 1)
                pe.wait_ge(onehot_ready, n + 1)
                for t in range(TILES):
                    for c in range(SPAN[u]):
                        last = nc.tensor.matmul(
                            turn_ps[:, u % 2].rearrange("p k b -> p (k b)")[:, t * PARTS * DIM:(t + 1) * PARTS * DIM],
                            onehot[:, u % RING, c, P * t:P * (t + 1)],
                            split_sb[:, SPAN_AT[u] + c].rearrange("p a d -> p (a d)"),
                            start=(c == 0), stop=(c == SPAN[u] - 1))
                last.then_inc(lookup_ready, 1)

            def gram_batch(s, k):
                pe.wait_ge(second_copied, GRAM_EMPTY + GRAM_BATCHES * s + k - 1)
                for u in range(BATCH_Q):
                    quad = BATCH_Q * k + u
                    t, q = u % TILES, (BATCH_Q * k + u) // TILES
                    e = emb_t[DIM * t:DIM * (t + 1), QUAD * q:QUAD * (q + 1), :]
                    last = nc.tensor.matmul(gram_ps[:, k % 2, t, u // TILES].rearrange("p h ij -> p (h ij)"),
                                            e.rearrange("p b f -> p (b f)"),
                                            e.rearrange("p b (h j) -> p h b j", h=2),
                                            start=True, stop=True)
                last.then_inc(gram_ready, 1)

            def layer1_tile(s, o, parity, turn):
                if o == 0:
                    pe.wait_ge(dense_placed[parity], 16 * CHUNKS * (turn + 1))
                if o == OT1 // 2:
                    pe.wait_ge(y_ready, Y_EMPTY + s)
                for jj in range(CHUNKS):
                    last = nc.tensor.matmul(mlp_ps[:, o // 2, o % 2, :], w1_sb[:, jj, P * o:P * (o + 1)],
                                            pairs[:, parity, :, jj, :], start=(jj == 0), stop=(jj == CHUNKS - 1))
                if o % 2:
                    last.then_inc(layer1_ready, 1)

            def layer2(s):
                for o in range(OT2):
                    for k in range(OT1):
                        if o == 0 and k != 1:
                            pe.wait_ge(h1_ready, OT1 * s + max(k + 1, 2))
                        last = nc.tensor.matmul(mlp_ps[:, 0, o, :], w2_sb[:, k, P * o:P * (o + 1)], h1[:, k, :],
                                                start=(k == 0), stop=(k == OT1 - 1))
                last.then_inc(layer2_ready, 1)

            def layer3(s):
                for k in range(OT2):
                    pe.wait_ge(h2_ready, OT2 * s + k + 1)
                    last = nc.tensor.matmul(mlp_ps[0:1, 1, 0, :], w3_sb[:, k:k + 1], h2[:, k, :],
                                            start=(k == 0), stop=(k == OT2 - 1))
                last.then_inc(layer3_ready, 1)

            def stay_warm(products):
                for _ in range(products):
                    nc.tensor.transpose(gram_ps[:, 0, 0].rearrange("p u h ij -> p (u h ij)")[:, 0:P],
                                        ident_sb[:], ident_sb[:])

            def step(s, parity, turn, mlp=True, ahead=True):
                for g in range(GROUPS):
                    if ahead:
                        for u in TURN_UNITS[g]:
                            look_up(s + 1, u)
                    if not ahead and g == GROUPS - 1:
                        pe.wait_ge(second_copied, GRAM_EMPTY + GRAM_BATCHES * s)
                        stay_warm(WARM_BEFORE)
                    transpose_group(s, parity, turn, g, 2 if ahead else 4)
                if not ahead:
                    stay_warm(WARM_AFTER)
                for k in range(GRAM_BATCHES):
                    if ahead:
                        for u in GRAM_UNITS[k]:
                            look_up(s + 1, u)
                    if k == 0:
                        if ahead:
                            pe.wait_ge(turned_drained, EMPTY + GROUPS * (s + 1))
                        else:
                            pe.wait_ge(turned_drained, EMPTY + GROUPS * s + GROUPS // 2)
                            pe.wait_ge(turned_by_dve, GROUPS // 2)
                    if mlp and k in LAYER1_BEFORE:
                        for o in range(OT1 // 2):
                            layer1_tile(s - 1, OT1 // 2 * LAYER1_BEFORE.index(k) + o, 1 - parity, turn - 1 + parity)
                    if mlp and k == LAYER2_BEFORE:
                        layer2(s - 1)
                    if mlp and k == LAYER3_BEFORE:
                        layer3(s - 1)
                    gram_batch(s, k)

            for u in range(UNITS):
                look_up(0, u, first=True)
            pe.wait_ge(ident_loaded, 16)
            step(0, 0, 0, mlp=False)
            pe.wait_ge(weights_loaded, 16 * WEIGHTS)
            with pe.Fori(0, SUPERS // 2 - 1) as pair:
                step(2 * pair + 1, 1, pair)
                step(2 * pair + 2, 0, pair + 1)
            step(SUPERS - 1, 1, SUPERS // 2 - 1, mlp=False, ahead=False)
            for s in (SUPERS - 2, SUPERS - 1):
                for o in range(OT1):
                    layer1_tile(s, o, s % 2, s // 2)
                layer2(s)
                layer3(s)

        def drain_turned(engine, copy, done, s, g, banks):
            engine.wait_ge(turned, GROUPS * s + g + 1)
            copy(emb_t[:, :, GROUP_F * g:GROUP_F * (g + 1)].rearrange("p b f -> p f b"),
                 turn_bank[g % banks]).then_inc(done, 1)

        def folded_batch(parity, k):
            return (folded[:, parity, :, :, BATCH_Q * k:BATCH_Q * (k + 1)]
                    .rearrange("p i j (q t) -> p t q (i j)", t=TILES))

        def part(u, which):
            return split_sb[:, SPAN_AT[u]:SPAN_AT[u + 1], which, :]

        def table_rows(u, flat):
            return flat[:, 0:SPAN[u] * DIM].rearrange("p (c d) -> p c d", d=DIM)

        @block.scalar
        def _(act):
            act.sem_inc(turned_drained, EMPTY)


            def layer1_half(s, half):
                act.wait_ge(layer1_ready, 2 * s + half + 1)
                for o in (2 * half, 2 * half + 1):
                    nc.scalar.activation(h1[:, o, :], mlp_ps[:, half, o % 2, :], ACT.Relu,
                                         bias=b1_sb[:, o:o + 1]).then_inc(h1_ready, 1)

            def convert(s, piece):
                if piece == 0:
                    act.wait_ge(ids32_loaded, 16 * (s + 1))
                us = slice(*PIECES[piece])
                nc.scalar.activation(place[:, us, :], ids32[:, us, :], ACT.Identity,
                                     bias=first_sb[:, piece:piece + 1]).then_inc(ids_converted, 1)

            def layer2_drain(s):
                act.wait_ge(layer2_ready, s + 1)
                for o in range(OT2):
                    nc.scalar.activation(h2[:, o, :], mlp_ps[:, 0, o, :], ACT.Relu,
                                         bias=b2_sb[:, o:o + 1]).then_inc(h2_ready, 1)

            def step(s, parity, mlp=True, ahead=True):
                for g in range(0, GROUPS, 1 if ahead else 2):
                    drain_turned(act, nc.scalar.copy, turned_drained, s, g, 2 if ahead else 4)
                for k in range(GRAM_BATCHES):
                    if mlp and k in LAYER1_BEFORE:
                        layer1_half(s - 1, LAYER1_BEFORE.index(k))
                    if mlp and k == LAYER2_BEFORE:
                        layer2_drain(s - 1)
                    if ahead and k in CONVERT_BEFORE:
                        convert(s + 2, CONVERT_BEFORE.index(k))
                    act.wait_ge(gram_ready, GRAM_BATCHES * s + k + 1)
                    nc.scalar.copy(folded_batch(parity, k),
                                   gram_ps[:, k % 2, :, :, 0, :]).then_inc(first_copied, 1)

            def high(u):
                act.wait_ge(whole_loaded[u], 16)
                nc.scalar.copy(part(u, 0), table_rows(u, whole[u])).then_inc(high_split, 1)

            def middle(u):
                act.wait_ge(high_taken, u + 1)
                nc.scalar.copy(part(u, 1), table_rows(u, residue[u % 2])).then_inc(middle_split, 1)

            high(0)
            high(1)
            act.wait_ge(first_loaded, 16)
            for piece in range(len(PIECES)):
                convert(0, piece)
            for u in range(UNITS):
                middle(u)
                if u + 2 < UNITS:
                    high(u + 2)
            for piece in range(len(PIECES)):
                if piece == len(PIECES) - 1:
                    act.wait_ge(onehot_ready, UNITS)
                convert(1, piece)
            step(0, 0, mlp=False)
            act.wait_ge(weights_loaded, 16 * WEIGHTS)
            with act.Fori(0, SUPERS // 2 - 1) as pair:
                step(2 * pair + 1, 1)
                step(2 * pair + 2, 0)
            step(SUPERS - 1, 1, mlp=False, ahead=False)
            for s in (SUPERS - 2, SUPERS - 1):
                layer1_half(s, 0)
                layer1_half(s, 1)
                layer2_drain(s)

        @block.vector
        def _(dve):
            dve.sem_inc(second_copied, GRAM_EMPTY)
            dve.sem_inc(y_ready, Y_EMPTY)

            def layer3_drain(s):
                dve.wait_ge(layer3_ready, s + 1)
                nc.vector.tensor_copy(
                    y[:, bass.ds(s * SUPER, SUPER)].rearrange("o (t q i) -> o i q t", i=QUAD, t=TILES),
                    mlp_ps[0:1, 1, 0, :].rearrange("o (i q t) -> o i q t", i=QUAD, t=TILES)).then_inc(y_ready, 1)

            def make_onehot(s, u):
                dve.wait_ge(ids_converted, len(PIECES) * s + PIECE_OF[u] + 1)
                for c in range(SPAN[u]):
                    last = nc.vector.tensor_scalar(onehot[:, u % RING, c, :], place[:, u, :],
                                                   float(c), None, ALU.is_equal)
                last.then_inc(onehot_ready, 1)

            def add_parts(s, u, parity):
                dve.wait_ge(lookup_ready, UNITS * s + u + 1)
                nc.vector.reduce_sum(
                    rows[:, parity, u, :, :],
                    turn_ps[:, u % 2].rearrange("p k b -> p (k b)")[:, 0:TILES * PARTS * DIM]
                    .rearrange("p (t a d) -> p t d a", t=TILES, a=PARTS), AX.X).then_inc(looked_up, 1)

            def follow(s, units, parity):
                for u in units:
                    add_parts(s, u, parity)
                    if u + READY_MADE < UNITS:
                        make_onehot(s, u + READY_MADE)

            def step(s, parity, mlp=True, ahead=True):
                if not ahead:
                    for g in range(1, GROUPS, 2):
                        drain_turned(dve, nc.vector.tensor_copy, turned_by_dve, s, g, 4)
                if ahead:
                    for g in range(GROUPS):
                        follow(s + 1, TURN_UNITS[g], 1 - parity)
                for k in range(GRAM_BATCHES):
                    if ahead:
                        follow(s + 1, GRAM_UNITS[k], 1 - parity)
                        if k >= GRAM_BATCHES - READY_MADE:
                            make_onehot(s + 2, k - (GRAM_BATCHES - READY_MADE))
                    if mlp and k == LAYER3_BEFORE:
                        layer3_drain(s - 1)
                    dve.wait_ge(first_copied, GRAM_BATCHES * s + k + 1)
                    dve.sem_inc(folds_begun, 1)
                    nc.vector.copy_predicated(
                        folded_batch(parity, k),
                        second_sb[:].unsqueeze(1).unsqueeze(1).to_broadcast([P, TILES, BATCH_Q // TILES, QUAD * HALF]),
                        gram_ps[:, k % 2, :, :, 1, :]).then_inc(second_copied, 1)

            def take_high(u):
                if u >= 2:
                    dve.wait_ge(table_split, u - 1)
                dve.wait_ge(high_split, u + 1)
                nc.vector.tensor_tensor(table_rows(u, residue[u % 2]), table_rows(u, whole[u]), part(u, 0),
                                        ALU.subtract).then_inc(high_taken, 1)

            def low(u):
                dve.wait_ge(middle_split, u + 1)
                nc.vector.tensor_tensor(part(u, 2), table_rows(u, residue[u % 2]), part(u, 1),
                                        ALU.subtract).then_inc(table_split, 1)

            take_high(0)
            for u in range(UNITS):
                if u >= RING:
                    add_parts(0, u - RING, 0)
                make_onehot(0, u)
                if u + 1 < UNITS:
                    take_high(u + 1)
                low(u)
            for u in range(UNITS - RING, UNITS):
                add_parts(0, u, 0)
            for u in range(READY_MADE):
                make_onehot(1, u)
            dve.wait_ge(second_loaded, 16)
            step(0, 0, mlp=False)
            with dve.Fori(0, SUPERS // 2 - 1) as pair:
                step(2 * pair + 1, 1)
                step(2 * pair + 2, 0)
            step(SUPERS - 1, 1, mlp=False, ahead=False)
            layer3_drain(SUPERS - 2)
            layer3_drain(SUPERS - 1)


def kernel(**inputs):
    import concourse.bacc as bacc
    from concourse.bass_utils import run_bass_kernel_spmd

    nc = bacc.Bacc("TRN2", target_bir_lowering=False, num_devices=1)
    arrays = {}

    def given(name, a):
        a = np.ascontiguousarray(a)
        arrays[name] = a
        return nc.dram_tensor(name, a.shape, mybir.dt.from_np(a.dtype), kind="ExternalInput").ap()

    rows, second = slot_meaning()
    x = {k: np.asarray(v) for k, v in inputs.items()}
    ids = given("ids", x["ids"])
    tables = [given(f"tbl_{f}", x[f"tbl_{f}"]) for f in range(FIELDS)]
    dense = given("dense", x["dense_ctx"].reshape(SUPERS, TILES, P // QUAD, QUAD, DENSE).transpose(0, 4, 3, 2, 1)
                  .reshape(SUPERS, DENSE, SUPER))
    w1 = given("w1", x["W_top1"][rows])
    b1 = given("b1", x["b_top1"].reshape(OT1, P).T)
    w2 = given("w2", x["W_top2"].reshape(OT1, P, HIDDEN2).transpose(1, 0, 2))
    b2 = given("b2", x["b_top2"].reshape(OT2, P).T)
    w3 = given("w3", x["W_top3"].reshape(OT2, P).T)
    identity = given("identity", np.eye(P, dtype=np.float32))
    second = given("second", second)
    looked_ids = x["ids"][:, LOOKED_UP].reshape(SUPERS, SUPER, UNITS).transpose(0, 2, 1)
    looked_ids = given("looked_ids", np.concatenate([looked_ids, looked_ids[-1:]]))
    first_rows = given("first_rows", np.stack([-SPAN[a] * np.arange(TP, dtype=np.float32) for a, _ in PIECES], axis=1))
    out = nc.dram_tensor("out", (BATCH, 1), mybir.dt.float32, kind="ExternalOutput").ap()
    build(nc, ids, tables, dense, w1, b1, w2, b2, w3, identity, second, looked_ids, first_rows, out)
    return run_bass_kernel_spmd(nc, [arrays], core_ids=[0]).results[0]["out"]
```
